# Optimizing a Trainium2 kernel written in Bass

```python
import numpy as np
import jax
import jax.numpy as jnp

def _softmax(x, axis=-1):
    return jax.nn.softmax(x, axis=axis)

def _gelu(x):
    return jax.nn.gelu(x, approximate=True)

def _silu(x):
    return jax.nn.silu(x)

def _sigmoid(x):
    return jax.nn.sigmoid(x)

def _layernorm(x, axis=-1, eps=1e-05):
    m = jnp.mean(x, axis=axis, keepdims=True)
    v = jnp.var(x, axis=axis, keepdims=True)
    return (x - m) / jnp.sqrt(v + eps)

def _scatter_add(tgt, idx, src, axis=0):
    return tgt.at[idx].add(src)

def _segment_sum(src, seg, n):
    return jax.ops.segment_sum(src, seg, n)
kernel_name = 'mk_rec_standalone_d1_rec_r8_21c91a'

def setup_inputs(seed: int=0):
    np.random.seed(seed)
    _w = jnp.asarray

    def _rec_inputs():
        import jax
        import jax.numpy as jnp
        _rk = jax.random.key(seed)
        r_dense = -0.00338568 + 1.0005 * jax.random.normal(jax.random.fold_in(_rk, 1), (512, 13), jnp.float32)
        r_sparse_idx = jnp.stack([jax.random.randint(jax.random.fold_in(jax.random.fold_in(_rk, 2), 0), (512,), 2, 12500, jnp.int32), jax.random.randint(jax.random.fold_in(jax.random.fold_in(_rk, 2), 1), (512,), 1, 99999, jnp.int32), jax.random.randint(jax.random.fold_in(jax.random.fold_in(_rk, 2), 2), (512,), 0, 12500, jnp.int32), jax.random.randint(jax.random.fold_in(jax.random.fold_in(_rk, 2), 3), (512,), 5, 12500, jnp.int32), jax.random.randint(jax.random.fold_in(jax.random.fold_in(_rk, 2), 4), (512,), 20, 99993, jnp.int32), jax.random.randint(jax.random.fold_in(jax.random.fold_in(_rk, 2), 5), (512,), 0, 99993, jnp.int32), jax.random.randint(jax.random.fold_in(jax.random.fold_in(_rk, 2), 6), (512,), 2, 99999, jnp.int32), jax.random.randint(jax.random.fold_in(jax.random.fold_in(_rk, 2), 7), (512,), 2, 99995, jnp.int32), jax.random.randint(jax.random.fold_in(jax.random.fold_in(_rk, 2), 8), (512,), 0, 99999, jnp.int32), jax.random.randint(jax.random.fold_in(jax.random.fold_in(_rk, 2), 9), (512,), 2, 99986, jnp.int32), jax.random.randint(jax.random.fold_in(jax.random.fold_in(_rk, 2), 10), (512,), 4, 99999, jnp.int32), jax.random.randint(jax.random.fold_in(jax.random.fold_in(_rk, 2), 11), (512,), 15, 99999, jnp.int32), jax.random.randint(jax.random.fold_in(jax.random.fold_in(_rk, 2), 12), (512,), 0, 99989, jnp.int32), jax.random.randint(jax.random.fold_in(jax.random.fold_in(_rk, 2), 13), (512,), 5, 99990, jnp.int32), jax.random.randint(jax.random.fold_in(jax.random.fold_in(_rk, 2), 14), (512,), 2, 99996, jnp.int32), jax.random.randint(jax.random.fold_in(jax.random.fold_in(_rk, 2), 15), (512,), 3, 99994, jnp.int32), jax.random.randint(jax.random.fold_in(jax.random.fold_in(_rk, 2), 16), (512,), 0, 99998, jnp.int32), jax.random.randint(jax.random.fold_in(jax.random.fold_in(_rk, 2), 17), (512,), 13, 99998, jnp.int32), jax.random.randint(jax.random.fold_in(jax.random.fold_in(_rk, 2), 18), (512,), 10, 12498, jnp.int32), jax.random.randint(jax.random.fold_in(jax.random.fold_in(_rk, 2), 19), (512,), 0, 99999, jnp.int32), jax.random.randint(jax.random.fold_in(jax.random.fold_in(_rk, 2), 20), (512,), 0, 99995, jnp.int32), jax.random.randint(jax.random.fold_in(jax.random.fold_in(_rk, 2), 21), (512,), 1, 99998, jnp.int32), jax.random.randint(jax.random.fold_in(jax.random.fold_in(_rk, 2), 22), (512,), 1, 99997, jnp.int32), jax.random.randint(jax.random.fold_in(jax.random.fold_in(_rk, 2), 23), (512,), 2, 99989, jnp.int32), jax.random.randint(jax.random.fold_in(jax.random.fold_in(_rk, 2), 24), (512,), 6, 12500, jnp.int32), jax.random.randint(jax.random.fold_in(jax.random.fold_in(_rk, 2), 25), (512,), 2, 99995, jnp.int32)], axis=1)
        return (r_dense, r_sparse_idx)
    r_dense, r_sparse_idx = _rec_inputs()

    def _L0_rec_setup():
        import jax, jax.numpy as jnp
        import numpy as np
        B, NF, D, V, NDENSE = (2048, 26, 64, 12500, 13)
        key = jax.random.key(seed)
        ks = jax.random.split(key, 16)
        s = 0.05
        return {'dense': jax.random.normal(ks[0], (B, NDENSE), jnp.float32), 'sparse_idx': jax.random.randint(ks[1], (B, NF), 0, V), 'emb_tables': jax.random.normal(ks[2], (NF, V, D), jnp.float32) * s, 'dw1': jax.random.normal(ks[3], (NDENSE, D), jnp.float32) * s, 'db1': jnp.zeros((D,), jnp.float32), 'dw2': jax.random.normal(ks[4], (D, D), jnp.float32) * s, 'db2': jnp.zeros((D,), jnp.float32), 'ow1': jax.random.normal(ks[5], ((NF + 1) * D + NF * (NF + 1) // 2, 512), jnp.float32) * s, 'ob1': jnp.zeros((512,), jnp.float32), 'ow2': jax.random.normal(ks[6], (512, 256), jnp.float32) * s, 'ob2': jnp.zeros((256,), jnp.float32), 'ow3': jax.random.normal(ks[7], (256, 128), jnp.float32) * s, 'ob3': jnp.zeros((128,), jnp.float32), 'ow4': jax.random.normal(ks[8], (128, 1), jnp.float32) * s, 'ob4': jnp.zeros((1,), jnp.float32)}
    _L0_rec_all = _L0_rec_setup()
    _L0_rec_in = {k: v for k, v in _L0_rec_all.items() if k in ('emb_tables', 'dw1', 'db1', 'dw2', 'db2', 'ow1', 'ob1', 'ow2', 'ob2', 'ow3', 'ob3', 'ow4', 'ob4')}
    del _L0_rec_all
    return {'r_dense': r_dense, 'r_sparse_idx': r_sparse_idx, 'L0_rec_emb_tables': _L0_rec_in['emb_tables'], 'L0_rec_dw1': _L0_rec_in['dw1'], 'L0_rec_db1': _L0_rec_in['db1'], 'L0_rec_dw2': _L0_rec_in['dw2'], 'L0_rec_db2': _L0_rec_in['db2'], 'L0_rec_ow1': _L0_rec_in['ow1'], 'L0_rec_ob1': _L0_rec_in['ob1'], 'L0_rec_ow2': _L0_rec_in['ow2'], 'L0_rec_ob2': _L0_rec_in['ob2'], 'L0_rec_ow3': _L0_rec_in['ow3'], 'L0_rec_ob3': _L0_rec_in['ob3'], 'L0_rec_ow4': _L0_rec_in['ow4'], 'L0_rec_ob4': _L0_rec_in['ob4']}

def reference(r_dense, r_sparse_idx, L0_rec_emb_tables, L0_rec_dw1, L0_rec_db1, L0_rec_dw2, L0_rec_db2, L0_rec_ow1, L0_rec_ob1, L0_rec_ow2, L0_rec_ob2, L0_rec_ow3, L0_rec_ob3, L0_rec_ow4, L0_rec_ob4):
    import jax
    import jax.numpy as jnp

    def _L0_rec_ref(dense, sparse_idx, emb_tables, dw1, db1, dw2, db2, ow1, ob1, ow2, ob2, ow3, ob3, ow4, ob4):
        import jax, jax.numpy as jnp
        import numpy as np
        B, NF, D, V, NDENSE = (2048, 26, 64, 12500, 13)
        h = jax.nn.relu(dense @ dw1 + db1)
        dense_emb = jax.nn.relu(h @ dw2 + db2)
        f_ids = jnp.arange(emb_tables.shape[0])[None, :]
        sparse_emb = emb_tables[f_ids, sparse_idx]
        emb = jnp.concatenate([dense_emb[:, None, :], sparse_emb], axis=1)
        inter = jnp.einsum('bfd,bgd->bfg', emb, emb)
        iu0, iu1 = jnp.triu_indices(emb.shape[1], k=1)
        pairs = inter[:, iu0, iu1]
        z = jnp.concatenate([emb.reshape(emb.shape[0], -1), pairs], axis=1)
        z = jax.nn.relu(z @ ow1 + ob1)
        z = jax.nn.relu(z @ ow2 + ob2)
        z = jax.nn.relu(z @ ow3 + ob3)
        return z @ ow4 + ob4
    y = _L0_rec_ref(r_dense, r_sparse_idx, L0_rec_emb_tables, L0_rec_dw1, L0_rec_db1, L0_rec_dw2, L0_rec_db2, L0_rec_ow1, L0_rec_ob1, L0_rec_ow2, L0_rec_ob2, L0_rec_ow3, L0_rec_ob3, L0_rec_ow4, L0_rec_ob4)
    return y

_drawn_inputs = setup_inputs


def setup_inputs(seed=0):
    import zlib

    import numpy as np

    out = dict(_drawn_inputs(seed))
    spreads = {'L0_rec_db1': (0.0, 0.1),
     'L0_rec_db2': (0.0, 0.1),
     'L0_rec_ob1': (0.0, 0.1),
     'L0_rec_ob2': (0.0, 0.1),
     'L0_rec_ob3': (0.0, 0.1)}
    factors = {}
    for name, (base, spread) in spreads.items():
        noise = np.random.default_rng([zlib.crc32(name.encode()), seed]).standard_normal(out[name].shape)
        drawn = base * np.exp(spread * noise) if base else spread * noise
        out[name] = jnp.asarray(drawn.astype(out[name].dtype))
    for name, factor in factors.items():
        out[name] = (out[name] * factor).astype(out[name].dtype)
    return out
```

```python
from contextlib import ExitStack

import concourse.bass as bass
from concourse import mybir

B = 512
NF = 26
V = 12500
D = 64
ND = 13
NE = NF + 1
H1, H2, H3 = 512, 256, 128

P = 128
TILES = B // P
FIELD_CHUNKS = NF // 2
QUAD = 32
QUAD_COLS = [(1, 7), (7, 13), (13, 20), (20, 27)]
SLOTS = 7
ONES_ROW = NE
CHUNKS = FIELD_CHUNKS + SLOTS
W_GROUP = 4
W_GROUPS = CHUNKS // W_GROUP
W_RING = 3
FREE_AT = {0: 4, 8: 8, 16: 12, 24: 13}
HALF = P // 2
GRPS = HALF // 4

DENSE_X, DENSE_W1, DENSE_W2, DENSE_B1, DENSE_B2 = 0, B, B + D, B + 2 * D, B + 2 * D + 1
DENSE_COLS = B + 2 * D + 2
IDENT, OW2, OW3 = 0, P, P + 4 * H2
OW4 = OW3 + 2 * H3
OB2, OB3, OB4 = OW4 + 1, OW4 + 3, OW4 + 4
SMALL_COLS = OW4 + 5

F32 = mybir.dt.float32
F32R = mybir.dt.float32r
I32 = mybir.dt.int32
ACT = mybir.ActivationFunctionType
ALU = mybir.AluOpType


def build(nc, idx, tables, dense_pack, small_pack, w1, out):
    with ExitStack() as ctx:
        def sb(name, shape, dt=F32):
            return ctx.enter_context(nc.sbuf_tensor(name, shape, dt))

        def ps(name, shape):
            return ctx.enter_context(nc.psum_tensor(name, shape, F32))

        def sem(name):
            return ctx.enter_context(nc.semaphore(name))

        idx_raw = sb("idx_raw", [P, TILES, NF], I32)
        idx_wrap = sb("idx_wrap", [P, TILES, NF], I32)
        idx_pos = sb("idx_pos", [P, TILES, NF], I32)
        idx_lim = sb("idx_lim", [P, TILES, NF], I32)
        table_base = sb("table_base", [P, TILES, NF], I32)
        rows = sb("rows", [P, TILES, NF], I32)
        tile_rows = sb("tile_rows", [P, 2, NF], I32)
        gathered = sb("gathered", [P, NF, D])
        dense_sb = sb("dense_sb", [D, DENSE_COLS])
        small = sb("small", [P, SMALL_COLS])
        dense_h = sb("dense_h", [D, B])
        dense_emb = sb("dense_emb", [D, B])
        w_raw = sb("w_raw", [P, W_RING, W_GROUP, H1])
        w_hi = sb("w_hi", [P, CHUNKS, H1], F32R)
        w_lo = sb("w_lo", [P, CHUNKS, H1], F32R)
        emb = sb("emb", [P, NE, P])
        x_hi = sb("x_hi", [P, FIELD_CHUNKS, P], F32R)
        x_lo = sb("x_lo", [P, FIELD_CHUNKS, P], F32R)
        pairs = sb("pairs", [P, SLOTS, P])
        p_hi = sb("p_hi", [P, SLOTS, P], F32R)
        p_lo = sb("p_lo", [P, SLOTS, P], F32R)
        z1 = sb("z1", [P, H1])
        z1t = sb("z1t", [P, H1 // P, P])
        z2t = sb("z2t", [P, H2 // P, P])
        z3t = sb("z3t", [P, P])
        y = sb("y", [1, B])

        ident = small[:, IDENT:IDENT + P]
        ow2 = small[:, OW2:OW2 + 4 * H2].rearrange("p (k n) -> p k n", k=4)
        ow3 = small[:, OW3:OW3 + 2 * H3].rearrange("p (k n) -> p k n", k=2)
        ow4 = small[:, OW4:OW4 + 1]

        turned = [ps(f"turned{i}", [P, 4 * P]) for i in range(2)]
        acc = ps("acc", [P, H1])
        inter = [ps(f"inter{i}", [P, 512]) for i in range(2)]
        bank_a, bank_b, bank_c = (ps(f"bank_{x}", [P, 512]) for x in "abc")
        dense_mm1, dense_mm2 = bank_a[0:D, :], bank_b[0:D, :]
        z1_turned = [bank_a[:, 0:2 * P], bank_b[:, 0:2 * P]]
        z2_ps = [bank_c[:, 0:P], bank_a[:, 0:P]]
        z3_ps = bank_b[:, 0:P]
        y_ps = bank_c[0:1, 0:P]

        idx_in = sem("idx_in")
        base_made = sem("base_made")
        idx_step = sem("idx_step")
        rows_ready = sem("rows_ready")
        rows_copied = sem("rows_copied")
        dense_in = sem("dense_in")
        small_in = sem("small_in")
        w_in = [sem(f"w_in{i}") for i in range(W_RING)]
        w_hi_done = sem("w_hi_done")
        w_lo_done = sem("w_lo_done")
        dense_mm = sem("dense_mm")
        dense_act = sem("dense_act")
        ones_set = sem("ones_set")
        chunk_in = [sem(f"chunk_in{c}") for c in range(FIELD_CHUNKS)]
        chunk_free = sem("chunk_free")
        hi_done = sem("hi_done")
        raw_done = sem("raw_done")
        pool_went_on = sem("pool_went_on")
        pe_went_on = sem("pe_went_on")
        lo_done = sem("lo_done")
        dense_placed = sem("dense_placed")
        inter_done = sem("inter_done")
        moved_act = sem("moved_act")
        moved_dve = sem("moved_dve")
        p_hi_done = sem("p_hi_done")
        p_lo_done = sem("p_lo_done")
        acc_done = sem("acc_done")
        z1_done = sem("z1_done")
        z1_turn = sem("z1_turn")
        z1t_done = sem("z1t_done")
        z2_mm = sem("z2_mm")
        z2_act = sem("z2_act")
        z2_dve = sem("z2_dve")
        z3_mm = sem("z3_mm")
        z3_act = sem("z3_act")
        y_mm = sem("y_mm")
        y_done = sem("y_done")
        y_out = sem("y_out")

        block = ctx.enter_context(nc.Block())

        def moved(k, j, q):
            lo, hi = QUAD_COLS[q]
            src = inter[k][QUAD * j:QUAD * j + NE, 0:GRPS * NF].rearrange("p (n g) -> p n g", g=NF)
            dst = pairs[QUAD * q:QUAD * q + NE, 0:hi - lo, HALF * k:HALF * (k + 1)]
            return src[:, :, lo - 1:hi - 1], dst.rearrange("p s (n j) -> p n s j", j=4)[:, :, :, j]

        SPLIT_SLOTS = [(0, 4), (4, SLOTS)]

        @block.sync
        def _(sp):
            sp.dma_start(idx_raw[:], idx).then_inc(idx_in, 16)
            for g in range(W_GROUPS):
                if g >= W_RING:
                    sp.wait_ge(w_lo_done, g - W_RING + 1)
                sp.dma_start(w_raw[:, g % W_RING], w1[:, g * W_GROUP:(g + 1) * W_GROUP, :]) \
                  .then_inc(w_in[g % W_RING], 16)
            sp.wait_ge(y_done, TILES)
            sp.dma_start(out, y[:]).then_inc(y_out, 16)
            sp.wait_ge(y_out, 16)

        @block.gpsimd
        def _(pool):
            nc.gpsimd.iota(table_base[:], pattern=[[0, TILES], [V, NF]], base=0,
                           channel_multiplier=0).then_inc(base_made, 1)
            pool.wait_ge(rows_ready, 1)
            with pool.Fori(0, TILES // 2) as pair:
                for half in range(2):
                    t = pair * 2 + half
                    nc.gpsimd.tensor_copy(tile_rows[:, half, :], rows[:, bass.ds(t, 1), :]) \
                      .then_inc(rows_copied, 1)
                    pool.wait_ge(rows_copied, t + 1)
                    for s in range(NF):
                        c = s // 2
                        if s in FREE_AT:
                            pool.wait_ge(chunk_free, t * FIELD_CHUNKS + FREE_AT[s])
                            pool.sem_inc(pool_went_on, 1)
                        pool.indirect_dma_start(
                            out=gathered[:, s, :], out_offset=None, in_=tables,
                            in_offset=bass.IndirectOffsetOnAxis(ap=tile_rows[:, half, s:s + 1], axis=0),
                        ).then_inc(chunk_in[c], 16)

        @block.tensor
        def _(pe):
            pe.sem_inc(chunk_free, FIELD_CHUNKS)

            pe.wait_ge(dense_in, 16)
            nc.tensor.matmul(dense_mm1, dense_sb[0:ND, DENSE_W1:DENSE_W1 + D],
                             dense_sb[0:ND, DENSE_X:DENSE_X + B], start=True, stop=True).then_inc(dense_mm, 1)
            pe.wait_ge(dense_act, 1)
            nc.tensor.matmul(dense_mm2, dense_sb[:, DENSE_W2:DENSE_W2 + D],
                             dense_h[:], start=True, stop=True).then_inc(dense_mm, 1)
            pe.wait_ge(small_in, 16)

            def product(hi, lo, chunk, first=False, last=False):
                nc.tensor.matmul(acc[:], hi, w_hi[:, chunk, :], start=first, stop=False)
                nc.tensor.matmul(acc[:], hi, w_lo[:, chunk, :], start=False, stop=False)
                return nc.tensor.matmul(acc[:], lo, w_hi[:, chunk, :], start=False, stop=last)

            with pe.Fori(0, TILES) as t:
                def field_product(c):
                    if c % W_GROUP == 0:
                        pe.wait_ge(w_lo_done, c // W_GROUP + 1)
                    pe.wait_ge(lo_done, t * FIELD_CHUNKS + c + 1)
                    product(x_hi[:, c, :], x_lo[:, c, :], c, first=(c == 0))

                for c in range(FIELD_CHUNKS):
                    bank = turned[c % 2]
                    pe.wait_ge(chunk_in[c], t * 32 + 32)
                    if c >= 2:
                        pe.wait_ge(raw_done, t * NF + 2 * (c - 1))
                    nc.tensor.transpose(bank[:, 0:P], gathered[:, 2 * c:2 * c + 2, :]
                                        .rearrange("p f d -> p (f d)"), ident)
                    nc.tensor.transpose(bank[0:D, P:2 * P], gathered[:, 2 * c + 1, :], ident) \
                      .then_inc(chunk_free, 1)
                    if c:
                        field_product(c - 1)
                field_product(FIELD_CHUNKS - 1)

                pe.wait_ge(raw_done, (t + 1) * NF)
                pe.wait_ge(dense_placed, t + 1)
                pe.sem_inc(pe_went_on, 1)
                for b in range(P):
                    k, j, n = b // HALF, b % 4, b % HALF // 4
                    mm = nc.tensor.matmul(inter[k][QUAD * j:QUAD * j + NE, n * NF:(n + 1) * NF],
                                          emb[0:D, :, b], emb[0:D, 1:NE, b], start=True, stop=True)
                    if b % HALF == HALF - 1:
                        mm.then_inc(inter_done, 1)

                for n, (lo, hi) in enumerate(SPLIT_SLOTS):
                    pe.wait_ge(p_lo_done, t * 2 + n + 1)
                    if n == 0:
                        pe.wait_ge(w_lo_done, W_GROUPS)
                    for s in range(lo, hi):
                        mm = product(p_hi[:, s, :], p_lo[:, s, :], FIELD_CHUNKS + s, last=(s == SLOTS - 1))
                mm.then_inc(acc_done, 1)

                for k in range(H1 // P):
                    if k % 2 == 0:
                        pe.wait_ge(z1_done, t * 2 + k // 2 + 1)
                    mm = nc.tensor.transpose(z1_turned[k // 2][:, k % 2 * P:(k % 2 + 1) * P],
                                             z1[:, k * P:(k + 1) * P], ident)
                    if k % 2:
                        mm.then_inc(z1_turn, 1)

                for m in range(H2 // P):
                    for k in range(H1 // P):
                        if m == 0 and k % 2 == 0:
                            pe.wait_ge(z1t_done, t * 2 + k // 2 + 1)
                        mm = nc.tensor.matmul(z2_ps[m], ow2[:, k, m * P:(m + 1) * P],
                                              z1t[:, k, :], start=(k == 0), stop=(k == H1 // P - 1))
                    mm.then_inc(z2_mm, 1)
                pe.wait_ge(z2_act, t + 1)
                nc.tensor.matmul(z3_ps, ow3[:, 0, :], z2t[:, 0, :], start=True, stop=False)
                pe.wait_ge(z2_dve, t + 1)
                nc.tensor.matmul(z3_ps, ow3[:, 1, :], z2t[:, 1, :], start=False, stop=True) \
                  .then_inc(z3_mm, 1)
                pe.wait_ge(z3_act, t + 1)
                nc.tensor.matmul(y_ps, ow4, z3t[:], start=True, stop=True).then_inc(y_mm, 1)

        @block.scalar
        def _(act):
            act.dma_start(dense_sb[:], dense_pack).then_inc(dense_in, 16)
            act.dma_start(small[:], small_pack).then_inc(small_in, 16)
            act.wait_ge(dense_mm, 1)
            nc.scalar.activation(dense_h[:], dense_mm1, ACT.Relu,
                                 bias=dense_sb[:, DENSE_B1:DENSE_B1 + 1]).then_inc(dense_act, 1)
            act.wait_ge(dense_mm, 2)
            nc.scalar.activation(dense_emb[:], dense_mm2, ACT.Relu,
                                 bias=dense_sb[:, DENSE_B2:DENSE_B2 + 1]).then_inc(dense_act, 1)
            for g in range(W_GROUPS):
                act.wait_ge(w_in[g % W_RING], 16 * (g // W_RING + 1))
                nc.scalar.activation(w_hi[:, g * W_GROUP:(g + 1) * W_GROUP, :], w_raw[:, g % W_RING],
                                     ACT.Copy).then_inc(w_hi_done, 1)
            act.wait_ge(small_in, 16)
            with act.Fori(0, TILES) as t:
                for c in range(FIELD_CHUNKS):
                    bank = turned[c % 2]
                    act.wait_ge(chunk_free, t * FIELD_CHUNKS + FIELD_CHUNKS + c + 1)
                    nc.scalar.activation(emb[:, 1 + 2 * c, :], bank[:, 0:P], ACT.Copy).then_inc(raw_done, 1)
                    nc.scalar.activation(emb[0:D, 2 + 2 * c, :], bank[0:D, P:2 * P], ACT.Copy).then_inc(raw_done, 1)
                for k in range(2):
                    act.wait_ge(inter_done, t * 2 + k + 1)
                    for j in range(2):
                        for q in range(4):
                            src, dst = moved(k, j, q)
                            last = nc.scalar.activation(dst, src, ACT.Copy)
                    last.then_inc(moved_act, 1)
                act.wait_ge(moved_act, t * 2 + 2)
                act.wait_ge(moved_dve, t * 2 + 2)
                for lo, hi in SPLIT_SLOTS:
                    nc.scalar.activation(p_hi[:, lo:hi, :], pairs[:, lo:hi, :], ACT.Copy).then_inc(p_hi_done, 1)
                act.wait_ge(acc_done, t + 1)
                for k in range(2):
                    half = slice(k * H1 // 2, (k + 1) * H1 // 2)
                    nc.scalar.activation(z1[:, half], acc[:, half], ACT.Relu).then_inc(z1_done, 1)
                act.wait_ge(z2_mm, t * 2 + 1)
                nc.scalar.activation(z2t[:, 0, :], z2_ps[0], ACT.Relu,
                                     bias=small[:, OB2:OB2 + 1]).then_inc(z2_act, 1)
                act.wait_ge(z3_mm, t + 1)
                nc.scalar.activation(z3t[:], z3_ps, ACT.Relu,
                                     bias=small[:, OB3:OB3 + 1]).then_inc(z3_act, 1)

        @block.vector
        def _(dve):
            dve.wait_ge(idx_in, 16)
            nc.vector.tensor_scalar(idx_wrap[:], idx_raw[:], 0, V, ALU.is_lt, ALU.mult).then_inc(idx_step, 1)
            dve.wait_ge(idx_step, 1)
            nc.vector.tensor_tensor(idx_pos[:], idx_raw[:], idx_wrap[:], ALU.add).then_inc(idx_step, 1)
            dve.wait_ge(idx_step, 2)
            nc.vector.tensor_scalar(idx_lim[:], idx_pos[:], 0, V - 1, ALU.max, ALU.min).then_inc(idx_step, 1)
            dve.wait_ge(idx_step, 3)
            dve.wait_ge(base_made, 1)
            nc.vector.tensor_tensor(rows[:], idx_lim[:], table_base[:], ALU.add).then_inc(rows_ready, 1)

            nc.vector.memset(pairs[:], 1.0).then_inc(ones_set, 1)
            for g in range(W_GROUPS):
                dve.wait_ge(w_hi_done, g + 1)
                part = slice(g * W_GROUP, (g + 1) * W_GROUP)
                nc.vector.tensor_tensor(w_lo[:, part, :], w_raw[:, g % W_RING], w_hi[:, part, :],
                                        ALU.subtract).then_inc(w_lo_done, 1)
            dve.wait_ge(dense_act, 2)
            dve.wait_ge(ones_set, 1)
            dve.wait_ge(small_in, 16)
            with dve.Fori(0, TILES) as t:
                tile = bass.ds(t * P, P)
                nc.vector.tensor_copy(emb[0:D, 0, :], dense_emb[:, tile])
                nc.vector.tensor_copy(pairs[0:D, SLOTS - 1, :], dense_emb[:, tile]).then_inc(dense_placed, 1)
                for c in range(FIELD_CHUNKS):
                    dve.wait_ge(raw_done, t * NF + 2 * c + 1)
                    nc.vector.tensor_copy(x_hi[:, c, :], emb[:, 1 + 2 * c, :]).then_inc(hi_done, 1)
                    dve.wait_ge(hi_done, t * FIELD_CHUNKS + c + 1)
                    nc.vector.tensor_tensor(x_lo[:, c, :], emb[:, 1 + 2 * c, :], x_hi[:, c, :],
                                            ALU.subtract).then_inc(lo_done, 1)
                for k in range(2):
                    dve.wait_ge(inter_done, t * 2 + k + 1)
                    for j in range(2, 4):
                        for q in range(4):
                            src, dst = moved(k, j, q)
                            last = nc.vector.tensor_copy(dst, src)
                    last.then_inc(moved_dve, 1)
                for n, (lo, hi) in enumerate(SPLIT_SLOTS):
                    dve.wait_ge(p_hi_done, t * 2 + n + 1)
                    nc.vector.tensor_tensor(p_lo[:, lo:hi, :], pairs[:, lo:hi, :], p_hi[:, lo:hi, :],
                                            ALU.subtract).then_inc(p_lo_done, 1)
                for k in range(2):
                    dve.wait_ge(z1_turn, t * 2 + k + 1)
                    nc.vector.tensor_copy(z1t[:, 2 * k:2 * k + 2, :],
                                          z1_turned[k].rearrange("p (k b) -> p k b", k=2)).then_inc(z1t_done, 1)
                dve.wait_ge(z2_mm, t * 2 + 2)
                nc.vector.tensor_scalar(z2t[:, 1, :], z2_ps[1], small[:, OB2 + 1:OB2 + 2], 0.0,
                                        ALU.add, ALU.max).then_inc(z2_dve, 1)
                dve.wait_ge(y_mm, t + 1)
                nc.vector.tensor_scalar(y[:, tile], y_ps, small[0:1, OB4:OB4 + 1], None,
                                        ALU.add).then_inc(y_done, 1)


def lay_out(inputs):
    import numpy as np

    def given(name):
        return np.asarray(inputs[name])

    ow1 = given("L0_rec_ow1")
    w1 = np.zeros((P, CHUNKS, H1), ow1.dtype)
    fields = ow1[D:NE * D].reshape(FIELD_CHUNKS, P, H1)
    w1[:, 0:FIELD_CHUNKS] = fields.transpose(1, 0, 2)
    for q, (lo, hi) in enumerate(QUAD_COLS):
        for g in range(lo, hi):
            for f in range(g):
                pair = NE * D + f * NE - f * (f + 1) // 2 + g - f - 1
                w1[QUAD * q + f, FIELD_CHUNKS + g - lo] = ow1[pair]
    w1[0:D, CHUNKS - 1] = ow1[0:D]
    w1[ONES_ROW, FIELD_CHUNKS] = given("L0_rec_ob1")

    dense_pack = np.zeros((D, DENSE_COLS), ow1.dtype)
    dense_pack[0:ND, DENSE_X:DENSE_X + B] = given("r_dense").T
    dense_pack[0:ND, DENSE_W1:DENSE_W1 + D] = given("L0_rec_dw1")
    dense_pack[:, DENSE_W2:DENSE_W2 + D] = given("L0_rec_dw2")
    dense_pack[:, DENSE_B1] = given("L0_rec_db1")
    dense_pack[:, DENSE_B2] = given("L0_rec_db2")

    small = np.zeros((P, SMALL_COLS), ow1.dtype)
    small[:, IDENT:IDENT + P] = np.eye(P, dtype=ow1.dtype)
    small[:, OW2:OW2 + 4 * H2] = given("L0_rec_ow2").reshape(4, P, H2).transpose(1, 0, 2).reshape(P, -1)
    small[:, OW3:OW3 + 2 * H3] = given("L0_rec_ow3").reshape(2, P, H3).transpose(1, 0, 2).reshape(P, -1)
    small[:, OW4:OW4 + 1] = given("L0_rec_ow4")
    small[:, OB2:OB2 + 2] = given("L0_rec_ob2").reshape(2, P).T
    small[:, OB3] = given("L0_rec_ob3")
    small[0, OB4] = given("L0_rec_ob4")[0]

    idx = given("r_sparse_idx").reshape(TILES, P, NF).transpose(1, 0, 2)
    return {
        "idx": np.ascontiguousarray(idx),
        "tables": given("L0_rec_emb_tables").reshape(NF * V, D),
        "dense_pack": dense_pack,
        "small_pack": small,
        "w1": w1,
    }


def kernel(**inputs):
    import concourse.bacc as bacc
    from concourse.bass_utils import run_bass_kernel_spmd

    nc = bacc.Bacc("TRN2", target_bir_lowering=False, num_devices=1)
    arrays = lay_out(inputs)
    args = [nc.dram_tensor(name, a.shape, mybir.dt.from_np(a.dtype), kind="ExternalInput").ap()
            for name, a in arrays.items()]
    out = nc.dram_tensor("out", (1, B), F32, kind="ExternalOutput").ap()
    build(nc, *args, out)
    got = run_bass_kernel_spmd(nc, [arrays], core_ids=[0])
    return got.results[0]["out"].reshape(B, 1)
```

```python
from contextlib import ExitStack

import concourse.bass as bass
from concourse import mybir

B = 512
NF = 26
V = 12500
D = 64
ND = 13
NE = NF + 1
H1, H2, H3 = 512, 256, 128

P = 128
TILES = B // P
FIELD_CHUNKS = NF // 2
QUAD = 32
SLOTS = 7
QUAD_SLOTS = [6, 6, 7, 7]
PLACES = 4 * SLOTS
DENSE_PLACE = SLOTS - 1
IDLE_PLACE = 2 * SLOTS - 1
SPARSE_PLACES = [SLOTS * q + s for q in range(4) for s in range(QUAD_SLOTS[q])]
ONES_ROW = PLACES
CHUNKS = FIELD_CHUNKS + SLOTS
W_FIRST = 4
W_GROUP = 2
W_GROUPS = CHUNKS // W_GROUP
W_RING = 5
FREE_AT = {0: 4, 8: 8, 16: 12, 24: 13}
HALF = P // 2
GRPS = HALF // 4
AHEAD = 5
LAG = 2
KEPT = 4
FIRST, LAST = 0, TILES - 1

DENSE_X, DENSE_W1, DENSE_W2, DENSE_B1, DENSE_B2 = 0, B, B + D, B + 2 * D, B + 2 * D + 1
DENSE_COLS = B + 2 * D + 2
IDENT, OW2, OW3 = 0, P, P + 4 * H2
OW4 = OW3 + 2 * H3
OB2, OB3, OB4 = OW4 + 1, OW4 + 3, OW4 + 4
SMALL_COLS = OW4 + 5

F32 = mybir.dt.float32
F32R = mybir.dt.float32r
I32 = mybir.dt.int32
ACT = mybir.ActivationFunctionType
ALU = mybir.AluOpType


def build(nc, idx, tables, dense_pack, small_pack, w1, out):
    with ExitStack() as ctx:
        def sb(name, shape, dt=F32):
            return ctx.enter_context(nc.sbuf_tensor(name, shape, dt))

        def ps(name, shape):
            return ctx.enter_context(nc.psum_tensor(name, shape, F32))

        def sem(name):
            return ctx.enter_context(nc.semaphore(name))

        idx_raw = sb("idx_raw", [P, TILES, NF], I32)
        idx_wrap = sb("idx_wrap", [P, TILES, NF], I32)
        idx_pos = sb("idx_pos", [P, TILES, NF], I32)
        idx_lim = sb("idx_lim", [P, TILES, NF], I32)
        table_base = sb("table_base", [P, TILES, NF], I32)
        rows = sb("rows", [P, TILES, NF], I32)
        tile_rows = sb("tile_rows", [P, 2, NF], I32)
        gathered = sb("gathered", [P, NF, D])
        dense_sb = sb("dense_sb", [D, DENSE_COLS])
        small = sb("small", [P, SMALL_COLS])
        dense_h = sb("dense_h", [D, B])
        dense_emb = sb("dense_emb", [D, B])
        w_raw = sb("w_raw", [P, W_RING, W_GROUP, H1])
        w_hi = sb("w_hi", [P, CHUNKS, H1], F32R)
        w_lo = sb("w_lo", [P, CHUNKS, H1], F32R)
        emb = sb("emb", [P, PLACES, P])
        x_hi = sb("x_hi", [P, FIELD_CHUNKS, P], F32R)
        x_lo = sb("x_lo", [P, FIELD_CHUNKS, P], F32R)
        pairs = sb("pairs", [P, SLOTS, P])
        p_hi = sb("p_hi", [P, SLOTS, P], F32R)
        p_lo = sb("p_lo", [P, SLOTS, P], F32R)
        z1 = sb("z1", [P, H1])
        z1t = sb("z1t", [P, H1 // P, P])
        z2t = sb("z2t", [P, H2 // P, P])
        z3t = sb("z3t", [P, P])
        y = sb("y", [1, B])

        ident = small[:, IDENT:IDENT + P]
        ow2 = small[:, OW2:OW2 + 4 * H2].rearrange("p (k n) -> p k n", k=4)
        ow3 = small[:, OW3:OW3 + 2 * H3].rearrange("p (k n) -> p k n", k=2)
        ow4 = small[:, OW4:OW4 + 1]

        turned = [ps(f"turned{i}", [P, 512]) for i in range(2)]
        acc = ps("acc", [P, H1])
        inter = [ps(f"inter{i}", [P, 512]) for i in range(2)]
        bank_a, bank_b = (ps(f"bank_{x}", [P, 512]) for x in "ab")
        dense_mm1, dense_mm2 = bank_a[0:D, :], bank_b[0:D, :]
        z1_turned = [bank_a[:, 0:2 * P], bank_b[:, 0:2 * P]]
        z2_ps = [bank_a[:, 0:P], bank_b[:, 0:P]]
        z3_ps = bank_a[:, 0:P]
        y_ps = bank_b[0:1, 0:P]

        idx_in = sem("idx_in")
        base_made = sem("base_made")
        idx_step = sem("idx_step")
        rows_ready = sem("rows_ready")
        rows_copied = sem("rows_copied")
        dense_in = sem("dense_in")
        small_in = sem("small_in")
        w_in = [sem(f"w_in{i}") for i in range(W_RING)]
        w_hi_done = sem("w_hi_done")
        w_lo_done = sem("w_lo_done")
        dense_mm = sem("dense_mm")
        dense_act = sem("dense_act")
        ones_set = sem("ones_set")
        chunk_in = [sem(f"chunk_in{c}") for c in range(FIELD_CHUNKS)]
        chunk_free = sem("chunk_free")
        hi_done = sem("hi_done")
        raw_done = sem("raw_done")
        pool_went_on = sem("pool_went_on")
        pe_went_on = sem("pe_went_on")
        lo_done = sem("lo_done")
        dense_placed = sem("dense_placed")
        inter_done = sem("inter_done")
        moved_act = sem("moved_act")
        moved_dve = sem("moved_dve")
        p_hi_done = sem("p_hi_done")
        p_lo_done = sem("p_lo_done")
        acc_done = sem("acc_done")
        z1_done = sem("z1_done")
        z1_turn = sem("z1_turn")
        z1t_done = sem("z1t_done")
        z2_mm = sem("z2_mm")
        z2_act = sem("z2_act")
        z2_dve = sem("z2_dve")
        z3_mm = sem("z3_mm")
        z3_act = sem("z3_act")
        y_mm = sem("y_mm")
        y_done = sem("y_done")
        y_out = sem("y_out")

        block = ctx.enter_context(nc.Block())

        SPLIT_SLOTS = [(0, 4), (4, SLOTS)]

        def place(s):
            return SPARSE_PLACES[s]

        def move(copy, k, quads):
            for j in quads:
                for q in range(4):
                    top = QUAD_SLOTS[q]
                    src = inter[k][QUAD * j:QUAD * j + PLACES, 0:GRPS * PLACES] \
                        .rearrange("p (n g) -> p n g", g=PLACES)[:, :, SLOTS * q:SLOTS * q + top]
                    dst = pairs[QUAD * q:QUAD * q + PLACES, 0:top, HALF * k:HALF * (k + 1)] \
                        .rearrange("p s (n j) -> p n s j", j=4)[:, :, :, j]
                    last = copy(dst, src)
            return last

        @block.sync
        def _(sp):
            sp.dma_start(idx_raw[:], idx).then_inc(idx_in, 16)
            for g in range(W_GROUPS):
                if g >= W_RING:
                    sp.wait_ge(w_lo_done, g - W_RING + 1)
                sp.dma_start(w_raw[:, g % W_RING], w1[:, g * W_GROUP:(g + 1) * W_GROUP, :]) \
                  .then_inc(w_in[g % W_RING], 16)
            sp.wait_ge(y_done, TILES)
            sp.dma_start(out, y[:]).then_inc(y_out, 16)
            sp.wait_ge(y_out, 16)

        @block.gpsimd
        def _(pool):
            nc.gpsimd.iota(table_base[:], pattern=[[0, TILES], [V, NF]], base=0,
                           channel_multiplier=0).then_inc(base_made, 1)
            pool.wait_ge(rows_ready, 1)
            with pool.Fori(0, TILES // 2) as pair:
                for half in range(2):
                    t = pair * 2 + half
                    nc.gpsimd.tensor_copy(tile_rows[:, half, :], rows[:, bass.ds(t, 1), :]) \
                      .then_inc(rows_copied, 1)
                    pool.wait_ge(rows_copied, t + 1)
                    for s in range(NF):
                        c = s // 2
                        if s in FREE_AT:
                            pool.wait_ge(chunk_free, t * FIELD_CHUNKS + FREE_AT[s])
                            pool.sem_inc(pool_went_on, 1)
                        pool.indirect_dma_start(
                            out=gathered[:, s, :], out_offset=None, in_=tables,
                            in_offset=bass.IndirectOffsetOnAxis(ap=tile_rows[:, half, s:s + 1], axis=0),
                        ).then_inc(chunk_in[c], 16)

        @block.tensor
        def _(pe):
            pe.sem_inc(chunk_free, FIELD_CHUNKS)

            pe.wait_ge(dense_in, 16)
            nc.tensor.matmul(dense_mm1, dense_sb[0:ND, DENSE_W1:DENSE_W1 + D],
                             dense_sb[0:ND, DENSE_X:DENSE_X + B], start=True, stop=True).then_inc(dense_mm, 1)
            pe.wait_ge(dense_act, 1)
            nc.tensor.matmul(dense_mm2, dense_sb[:, DENSE_W2:DENSE_W2 + D],
                             dense_h[:], start=True, stop=True).then_inc(dense_mm, 1)
            pe.wait_ge(small_in, 16)

            def product(hi, lo, chunk, first=False, last=False):
                nc.tensor.matmul(acc[:], hi, w_hi[:, chunk, :], start=first, stop=False)
                nc.tensor.matmul(acc[:], hi, w_lo[:, chunk, :], start=False, stop=False)
                return nc.tensor.matmul(acc[:], lo, w_hi[:, chunk, :], start=False, stop=last)

            def turn(t, c):
                pe.wait_ge(chunk_in[c], t * 32 + 32)
                if c >= 2:
                    pe.wait_ge(raw_done, t * NF + 2 * (c - 1))
                nc.tensor.transpose(turned[c % 2][:, 0:P], gathered[:, 2 * c:2 * c + 2, :]
                                    .rearrange("p f d -> p (f d)"), ident).then_inc(chunk_free, 1)

            def field_product(t, c):
                if c % W_GROUP == 0:
                    pe.wait_ge(w_lo_done, c // W_GROUP + 1)
                pe.wait_ge(lo_done, t * FIELD_CHUNKS + c + 1)
                product(x_hi[:, c, :], x_lo[:, c, :], c, first=(c == 0))

            def interactions(t):
                pe.wait_ge(raw_done, (t + 1) * NF)
                pe.wait_ge(dense_placed, t + 1)
                pe.sem_inc(pe_went_on, 1)
                for b in range(P):
                    k, j, n = b // HALF, b % 4, b % HALF // 4
                    mm = nc.tensor.matmul(inter[k][QUAD * j:QUAD * j + PLACES, n * PLACES:(n + 1) * PLACES],
                                          emb[0:D, :, b], emb[0:D, :, b], start=True, stop=True)
                    if b % HALF == HALF - 1:
                        mm.then_inc(inter_done, 1)

            def pair_product(t, part):
                pe.wait_ge(p_lo_done, t * 2 + part + 1)
                pe.wait_ge(w_lo_done, W_GROUPS)
                for s in range(*SPLIT_SLOTS[part]):
                    mm = product(p_hi[:, s, :], p_lo[:, s, :], FIELD_CHUNKS + s, last=(s == SLOTS - 1))
                if part:
                    mm.then_inc(acc_done, 1)

            def z1_to_features(t):
                for k in range(H1 // P):
                    if k % 2 == 0:
                        pe.wait_ge(z1_done, t * 2 + k // 2 + 1)
                    mm = nc.tensor.transpose(z1_turned[k // 2][:, k % 2 * P:(k % 2 + 1) * P],
                                             z1[:, k * P:(k + 1) * P], ident)
                    if k % 2:
                        mm.then_inc(z1_turn, 1)

            def layer2(t):
                for m in range(H2 // P):
                    for k in range(H1 // P):
                        if m == 0 and k % 2 == 0:
                            pe.wait_ge(z1t_done, t * 2 + k // 2 + 1)
                        mm = nc.tensor.matmul(z2_ps[m], ow2[:, k, m * P:(m + 1) * P],
                                              z1t[:, k, :], start=(k == 0), stop=(k == H1 // P - 1))
                    mm.then_inc(z2_mm, 1)

            def layer3(t):
                pe.wait_ge(z2_act, t + 1)
                nc.tensor.matmul(z3_ps, ow3[:, 0, :], z2t[:, 0, :], start=True, stop=False)
                pe.wait_ge(z2_dve, t + 1)
                nc.tensor.matmul(z3_ps, ow3[:, 1, :], z2t[:, 1, :], start=False, stop=True) \
                  .then_inc(z3_mm, 1)

            def layer4(t):
                pe.wait_ge(z3_act, t + 1)
                nc.tensor.matmul(y_ps, ow4, z3t[:], start=True, stop=True).then_inc(y_mm, 1)

            for c in range(AHEAD):
                turn(0, c)
                if c >= LAG:
                    field_product(0, c - LAG)
            for c in range(AHEAD - LAG, AHEAD):
                field_product(0, c)
            with pe.Fori(0, LAST) as t:
                for c in range(AHEAD, FIELD_CHUNKS):
                    turn(t, c)
                    if AHEAD <= c - LAG < FIELD_CHUNKS - KEPT:
                        field_product(t, c - LAG)
                interactions(t)
                for c in range(FIELD_CHUNKS - KEPT, FIELD_CHUNKS):
                    field_product(t, c)
                turn(t + 1, 0)
                turn(t + 1, 1)
                pair_product(t, 0)
                turn(t + 1, 2)
                pair_product(t, 1)
                turn(t + 1, 3)
                z1_to_features(t)
                field_product(t + 1, 0)
                turn(t + 1, 4)
                field_product(t + 1, 1)
                layer2(t)
                field_product(t + 1, 2)
                layer3(t)
                field_product(t + 1, 3)
                layer4(t)
                field_product(t + 1, 4)
            for c in range(AHEAD, FIELD_CHUNKS):
                turn(LAST, c)
                if AHEAD <= c - LAG < FIELD_CHUNKS - KEPT:
                    field_product(LAST, c - LAG)
            interactions(LAST)
            for c in range(FIELD_CHUNKS - KEPT, FIELD_CHUNKS):
                field_product(LAST, c)
            pair_product(LAST, 0)
            pair_product(LAST, 1)
            z1_to_features(LAST)
            layer2(LAST)
            layer3(LAST)
            layer4(LAST)

        @block.scalar
        def _(act):
            act.dma_start(dense_sb[:], dense_pack).then_inc(dense_in, 16)
            act.dma_start(small[:], small_pack).then_inc(small_in, 16)
            act.wait_ge(dense_mm, 1)
            nc.scalar.activation(dense_h[:], dense_mm1, ACT.Relu,
                                 bias=dense_sb[:, DENSE_B1:DENSE_B1 + 1]).then_inc(dense_act, 1)
            act.wait_ge(dense_mm, 2)
            nc.scalar.activation(dense_emb[:], dense_mm2, ACT.Relu,
                                 bias=dense_sb[:, DENSE_B2:DENSE_B2 + 1]).then_inc(dense_act, 1)

            def weights_hi(g):
                act.wait_ge(w_in[g % W_RING], 16 * (g // W_RING + 1))
                nc.scalar.activation(w_hi[:, g * W_GROUP:(g + 1) * W_GROUP, :], w_raw[:, g % W_RING],
                                     ACT.Copy).then_inc(w_hi_done, 1)

            for g in range(W_FIRST):
                weights_hi(g)
            act.wait_ge(small_in, 16)

            def raw(t, c):
                bank = turned[c % 2]
                act.wait_ge(chunk_free, t * FIELD_CHUNKS + FIELD_CHUNKS + c + 1)
                nc.scalar.activation(emb[:, place(2 * c), :], bank[:, 0:P], ACT.Copy).then_inc(raw_done, 1)
                nc.scalar.activation(emb[0:D, place(2 * c + 1), :], bank[D:P, 0:P], ACT.Copy) \
                  .then_inc(raw_done, 1)

            def moves(t):
                for k in range(2):
                    act.wait_ge(inter_done, t * 2 + k + 1)
                    move(lambda dst, src: nc.scalar.activation(dst, src, ACT.Copy), k, (0, 1)) \
                        .then_inc(moved_act, 1)
                act.wait_ge(moved_act, t * 2 + 2)
                act.wait_ge(moved_dve, t * 2 + 2)

            def pairs_hi(part):
                part = slice(*SPLIT_SLOTS[part])
                nc.scalar.activation(p_hi[:, part, :], pairs[:, part, :], ACT.Copy).then_inc(p_hi_done, 1)

            def z1_relu(t):
                act.wait_ge(acc_done, t + 1)
                for k in range(2):
                    half = slice(k * H1 // 2, (k + 1) * H1 // 2)
                    nc.scalar.activation(z1[:, half], acc[:, half], ACT.Relu).then_inc(z1_done, 1)

            def z2_z3_relu(t):
                act.wait_ge(z2_mm, t * 2 + 1)
                nc.scalar.activation(z2t[:, 0, :], z2_ps[0], ACT.Relu,
                                     bias=small[:, OB2:OB2 + 1]).then_inc(z2_act, 1)
                act.wait_ge(z3_mm, t + 1)
                nc.scalar.activation(z3t[:], z3_ps, ACT.Relu,
                                     bias=small[:, OB3:OB3 + 1]).then_inc(z3_act, 1)

            for c in range(AHEAD):
                raw(0, c)
            for g in range(W_FIRST, W_GROUPS):
                weights_hi(g)
            with act.Fori(0, LAST) as t:
                for c in range(AHEAD, FIELD_CHUNKS):
                    raw(t, c)
                moves(t)
                pairs_hi(0)
                pairs_hi(1)
                for c in range(3):
                    raw(t + 1, c)
                z1_relu(t)
                for c in range(3, AHEAD):
                    raw(t + 1, c)
                z2_z3_relu(t)
            for c in range(AHEAD, FIELD_CHUNKS):
                raw(LAST, c)
            moves(LAST)
            pairs_hi(0)
            pairs_hi(1)
            z1_relu(LAST)
            z2_z3_relu(LAST)

        @block.vector
        def _(dve):
            dve.wait_ge(idx_in, 16)
            nc.vector.tensor_scalar(idx_wrap[:], idx_raw[:], 0, V, ALU.is_lt, ALU.mult).then_inc(idx_step, 1)
            dve.wait_ge(idx_step, 1)
            nc.vector.tensor_tensor(idx_pos[:], idx_raw[:], idx_wrap[:], ALU.add).then_inc(idx_step, 1)
            dve.wait_ge(idx_step, 2)
            nc.vector.tensor_scalar(idx_lim[:], idx_pos[:], 0, V - 1, ALU.max, ALU.min).then_inc(idx_step, 1)
            dve.wait_ge(idx_step, 3)
            dve.wait_ge(base_made, 1)
            nc.vector.tensor_tensor(rows[:], idx_lim[:], table_base[:], ALU.add).then_inc(rows_ready, 1)

            nc.vector.memset(pairs[:], 1.0).then_inc(ones_set, 1)
            nc.vector.memset(emb[:, IDLE_PLACE, :], 0.0).then_inc(ones_set, 1)

            def weights_lo(g):
                dve.wait_ge(w_hi_done, g + 1)
                part = slice(g * W_GROUP, (g + 1) * W_GROUP)
                nc.vector.tensor_tensor(w_lo[:, part, :], w_raw[:, g % W_RING], w_hi[:, part, :],
                                        ALU.subtract).then_inc(w_lo_done, 1)

            for g in range(W_FIRST):
                weights_lo(g)
            dve.wait_ge(dense_act, 2)
            dve.wait_ge(ones_set, 2)
            dve.wait_ge(small_in, 16)

            def dense_place(t):
                tile = bass.ds(t * P, P)
                if t is not FIRST:
                    dve.wait_ge(p_lo_done, t * 2)
                nc.vector.tensor_copy(emb[0:D, DENSE_PLACE, :], dense_emb[:, tile])
                nc.vector.tensor_copy(pairs[0:D, SLOTS - 1, :], dense_emb[:, tile]).then_inc(dense_placed, 1)

            def split(t, c):
                x = emb[:, place(2 * c), :]
                dve.wait_ge(raw_done, t * NF + 2 * c + 1)
                nc.vector.tensor_copy(x_hi[:, c, :], x).then_inc(hi_done, 1)
                dve.wait_ge(hi_done, t * FIELD_CHUNKS + c + 1)
                nc.vector.tensor_tensor(x_lo[:, c, :], x, x_hi[:, c, :], ALU.subtract).then_inc(lo_done, 1)

            def moves(t):
                for k in range(2):
                    dve.wait_ge(inter_done, t * 2 + k + 1)
                    move(nc.vector.tensor_copy, k, (2, 3)).then_inc(moved_dve, 1)

            def pairs_lo(t, part):
                dve.wait_ge(p_hi_done, t * 2 + part + 1)
                part = slice(*SPLIT_SLOTS[part])
                nc.vector.tensor_tensor(p_lo[:, part, :], pairs[:, part, :], p_hi[:, part, :],
                                        ALU.subtract).then_inc(p_lo_done, 1)

            def z1_features(t):
                for k in range(2):
                    dve.wait_ge(z1_turn, t * 2 + k + 1)
                    nc.vector.tensor_copy(z1t[:, 2 * k:2 * k + 2, :],
                                          z1_turned[k].rearrange("p (k b) -> p k b", k=2)).then_inc(z1t_done, 1)

            def z2_and_y(t):
                dve.wait_ge(z2_mm, t * 2 + 2)
                nc.vector.tensor_scalar(z2t[:, 1, :], z2_ps[1], small[:, OB2 + 1:OB2 + 2], 0.0,
                                        ALU.add, ALU.max).then_inc(z2_dve, 1)
                dve.wait_ge(y_mm, t + 1)
                nc.vector.tensor_scalar(y[:, bass.ds(t * P, P)], y_ps, small[0:1, OB4:OB4 + 1], None,
                                        ALU.add).then_inc(y_done, 1)

            dense_place(FIRST)
            for c in range(AHEAD):
                split(0, c)
            for g in range(W_FIRST, W_GROUPS):
                weights_lo(g)
            with dve.Fori(0, LAST) as t:
                for c in range(AHEAD, FIELD_CHUNKS):
                    split(t, c)
                moves(t)
                pairs_lo(t, 0)
                pairs_lo(t, 1)
                dense_place(t + 1)
                for c in range(3):
                    split(t + 1, c)
                z1_features(t)
                for c in range(3, AHEAD):
                    split(t + 1, c)
                z2_and_y(t)
            for c in range(AHEAD, FIELD_CHUNKS):
                split(LAST, c)
            moves(LAST)
            pairs_lo(LAST, 0)
            pairs_lo(LAST, 1)
            z1_features(LAST)
            z2_and_y(LAST)


def lay_out(inputs):
    import numpy as np

    def given(name):
        return np.asarray(inputs[name])

    ow1 = given("L0_rec_ow1")
    w1 = np.zeros((P, CHUNKS, H1), ow1.dtype)
    fields = ow1[D:NE * D].reshape(FIELD_CHUNKS, P, H1)
    w1[:, 0:FIELD_CHUNKS] = fields.transpose(1, 0, 2)
    places = [DENSE_PLACE, *SPARSE_PLACES]
    for g in range(1, NE):
        q, slot = divmod(places[g], SLOTS)
        for f in range(g):
            pair = NE * D + f * NE - f * (f + 1) // 2 + g - f - 1
            w1[QUAD * q + places[f], FIELD_CHUNKS + slot] = ow1[pair]
    w1[0:D, CHUNKS - 1] = ow1[0:D]
    w1[ONES_ROW, FIELD_CHUNKS] = given("L0_rec_ob1")

    dense_pack = np.zeros((D, DENSE_COLS), ow1.dtype)
    dense_pack[0:ND, DENSE_X:DENSE_X + B] = given("r_dense").T
    dense_pack[0:ND, DENSE_W1:DENSE_W1 + D] = given("L0_rec_dw1")
    dense_pack[:, DENSE_W2:DENSE_W2 + D] = given("L0_rec_dw2")
    dense_pack[:, DENSE_B1] = given("L0_rec_db1")
    dense_pack[:, DENSE_B2] = given("L0_rec_db2")

    small = np.zeros((P, SMALL_COLS), ow1.dtype)
    small[:, IDENT:IDENT + P] = np.eye(P, dtype=ow1.dtype)
    small[:, OW2:OW2 + 4 * H2] = given("L0_rec_ow2").reshape(4, P, H2).transpose(1, 0, 2).reshape(P, -1)
    small[:, OW3:OW3 + 2 * H3] = given("L0_rec_ow3").reshape(2, P, H3).transpose(1, 0, 2).reshape(P, -1)
    small[:, OW4:OW4 + 1] = given("L0_rec_ow4")
    small[:, OB2:OB2 + 2] = given("L0_rec_ob2").reshape(2, P).T
    small[:, OB3] = given("L0_rec_ob3")
    small[0, OB4] = given("L0_rec_ob4")[0]

    idx = given("r_sparse_idx").reshape(TILES, P, NF).transpose(1, 0, 2)
    return {
        "idx": np.ascontiguousarray(idx),
        "tables": given("L0_rec_emb_tables").reshape(NF * V, D),
        "dense_pack": dense_pack,
        "small_pack": small,
        "w1": w1,
    }


def kernel(**inputs):
    import concourse.bacc as bacc
    from concourse.bass_utils import run_bass_kernel_spmd

    nc = bacc.Bacc("TRN2", target_bir_lowering=False, num_devices=1)
    arrays = lay_out(inputs)
    args = [nc.dram_tensor(name, a.shape, mybir.dt.from_np(a.dtype), kind="ExternalInput").ap()
            for name, a in arrays.items()]
    out = nc.dram_tensor("out", (1, B), F32, kind="ExternalOutput").ap()
    build(nc, *args, out)
    got = run_bass_kernel_spmd(nc, [arrays], core_ids=[0])
    return got.results[0]["out"].reshape(B, 1)
```

```python
from contextlib import ExitStack

import concourse.bass as bass
from concourse import mybir

B = 512
NF = 26
V = 12500
D = 64
ND = 13
NE = NF + 1
H1, H2, H3 = 512, 256, 128

P = 128
TILES = B // P
FIELD_CHUNKS = NF // 2
QUAD = 32
SLOTS = 7
QUAD_SLOTS = [6, 6, 7, 7]
PLACES = 4 * SLOTS
DENSE_PLACE = SLOTS - 1
IDLE_PLACE = 2 * SLOTS - 1
SPARSE_PLACES = [SLOTS * q + s for q in range(4) for s in range(QUAD_SLOTS[q])]
ONES_ROW = PLACES
CHUNKS = FIELD_CHUNKS + SLOTS
W_FIRST = 4
W_GROUP = 2
W_GROUPS = CHUNKS // W_GROUP
W_RING = 5
FREE_AT = {0: 8, 16: FIELD_CHUNKS}
BANK_FROM = [0, 72, P]
AHEAD = 5
LAYER2_AT = {9: (0, 1), 11: (2,)}
LAG = 2
FIRST, LAST = 0, TILES - 1
SPLIT_SLOTS = [(0, 1), (1, 4), (4, SLOTS)]
PARTS = len(SPLIT_SLOTS)
Z1_STEPS = [(0, 1), (1, 2), (2, 4)]
STEPS = len(Z1_STEPS)
LAYER2_STEPS = [[(0, 0)], [(0, 1), (1, 0), (1, 1)], [(0, 2), (0, 3), (1, 2), (1, 3)]]

DENSE_X, DENSE_W1, DENSE_W2, DENSE_B1, DENSE_B2 = 0, B, B + D, B + 2 * D, B + 2 * D + 1
DENSE_COLS = B + 2 * D + 2
IDENT, OW2, OW3 = 0, P, P + 4 * H2
OW4 = OW3 + 2 * H3
OB2, OB3, OB4 = OW4 + 1, OW4 + 3, OW4 + 4
SMALL_COLS = OW4 + 5

F32 = mybir.dt.float32
F32R = mybir.dt.float32r
I32 = mybir.dt.int32
ACT = mybir.ActivationFunctionType
ALU = mybir.AluOpType


def build(nc, idx, tables, dense_pack, small_pack, w1, out):
    with ExitStack() as ctx:
        def sb(name, shape, dt=F32):
            return ctx.enter_context(nc.sbuf_tensor(name, shape, dt))

        def ps(name, shape):
            return ctx.enter_context(nc.psum_tensor(name, shape, F32))

        def sem(name):
            return ctx.enter_context(nc.semaphore(name))

        idx_raw = sb("idx_raw", [P, TILES, NF], I32)
        idx_wrap = sb("idx_wrap", [P, TILES, NF], I32)
        idx_pos = sb("idx_pos", [P, TILES, NF], I32)
        table_base = sb("table_base", [P, TILES, NF], I32)
        rows = sb("rows", [P, TILES, NF], I32)
        tile_rows = sb("tile_rows", [P, 2, NF], I32)
        gathered = sb("gathered", [P, NF, D])
        dense_sb = sb("dense_sb", [D, DENSE_COLS])
        small = sb("small", [P, SMALL_COLS])
        dense_h = sb("dense_h", [D, B])
        dense_emb = sb("dense_emb", [D, B])
        w_raw = sb("w_raw", [P, W_RING, W_GROUP, H1])
        w_hi = sb("w_hi", [P, CHUNKS, H1], F32R)
        w_lo = sb("w_lo", [P, CHUNKS, H1], F32R)
        emb = sb("emb", [P, PLACES, P])
        x_hi = sb("x_hi", [P, FIELD_CHUNKS, P], F32R)
        x_lo = sb("x_lo", [P, FIELD_CHUNKS, P], F32R)
        pairs = sb("pairs", [P, SLOTS, P])
        p_hi = sb("p_hi", [P, SLOTS, P], F32R)
        p_lo = sb("p_lo", [P, SLOTS, P], F32R)
        z1 = sb("z1", [P, H1])
        z1t = sb("z1t", [P, H1 // P, P])
        z2t = sb("z2t", [P, H2 // P, P])
        z3t = sb("z3t", [P, P])
        y = sb("y", [1, B])

        ident = small[:, IDENT:IDENT + P]
        ow2 = small[:, OW2:OW2 + 4 * H2].rearrange("p (k n) -> p k n", k=4)
        ow3 = small[:, OW3:OW3 + 2 * H3].rearrange("p (k n) -> p k n", k=2)
        ow4 = small[:, OW4:OW4 + 1]

        turned = [ps(f"turned{i}", [P, 512]) for i in range(2)]
        acc = ps("acc", [P, H1])
        inter = [ps(f"inter{i}", [P, 512]) for i in range(2)]
        bank_a, bank_b, bank_c = (ps(f"bank_{x}", [P, 512]) for x in "abc")
        dense_mm1, dense_mm2 = bank_a[0:D, :], bank_b[0:D, :]
        z1_turned = [bank_a[:, 0:P], bank_b[:, 0:P], bank_c[:, 0:2 * P]]
        z2_ps = [bank_a[:, 0:P], bank_b[:, 0:P]]
        z3_ps = inter[0][:, 0:P]
        y_ps = inter[1][0:1, 0:P]

        idx_in = sem("idx_in")
        later_idx_in = sem("later_idx_in")
        base_made = sem("base_made")
        idx_step = sem("idx_step")
        rows_ready = sem("rows_ready")
        rows_done = sem("rows_done")
        dense_in = sem("dense_in")
        small_in = sem("small_in")
        w_in = [sem(f"w_in{i}") for i in range(W_RING)]
        w_hi_done = sem("w_hi_done")
        w_lo_done = sem("w_lo_done")
        dense_mm = sem("dense_mm")
        dense_act = sem("dense_act")
        ones_set = sem("ones_set")
        chunk_in = [sem(f"chunk_in{c}") for c in range(FIELD_CHUNKS)]
        chunk_free = sem("chunk_free")
        x_hi_done = sem("x_hi_done")
        emb_done = sem("emb_done")
        pool_went_on = sem("pool_went_on")
        pe_went_on = sem("pe_went_on")
        x_lo_done = sem("x_lo_done")
        dense_placed = sem("dense_placed")
        inter_done = sem("inter_done")
        moved_act = sem("moved_act")
        moved_dve = sem("moved_dve")
        p_hi_done = sem("p_hi_done")
        p_lo_done = sem("p_lo_done")
        acc_done = sem("acc_done")
        z1_done = sem("z1_done")
        z1_turn = sem("z1_turn")
        z1t_done = sem("z1t_done")
        z2_mm = sem("z2_mm")
        z2_act = sem("z2_act")
        z2_dve = sem("z2_dve")
        z3_mm = sem("z3_mm")
        z3_act = sem("z3_act")
        y_mm = sem("y_mm")
        y_done = sem("y_done")
        y_out = sem("y_out")

        block = ctx.enter_context(nc.Block())

        def place(s):
            return SPARSE_PLACES[s]

        def move(copy, k, quads):
            b0, b1 = BANK_FROM[k:k + 2]
            for j in quads:
                for q in range(4):
                    top = QUAD_SLOTS[q]
                    src = inter[k][QUAD * j:QUAD * j + PLACES, 0:(b1 - b0) // 4 * PLACES] \
                        .rearrange("p (n g) -> p n g", g=PLACES)[:, :, SLOTS * q:SLOTS * q + top]
                    dst = pairs[QUAD * q:QUAD * q + PLACES, 0:top, b0:b1] \
                        .rearrange("p s (n j) -> p n s j", j=4)[:, :, :, j]
                    last = copy(dst, src)
            return last

        @block.sync
        def _(sp):
            sp.dma_start(idx_raw[:, 0:1, :], idx[:, 0:1, :]).then_inc(idx_in, 16)
            sp.dma_start(idx_raw[:, 1:TILES, :], idx[:, 1:TILES, :]).then_inc(later_idx_in, 16)
            for g in range(W_GROUPS):
                if g >= W_RING:
                    sp.wait_ge(w_lo_done, g - W_RING + 1)
                sp.dma_start(w_raw[:, g % W_RING], w1[:, g * W_GROUP:(g + 1) * W_GROUP, :]) \
                  .then_inc(w_in[g % W_RING], 16)
            sp.wait_ge(y_done, TILES)
            sp.dma_start(out, y[:]).then_inc(y_out, 16)
            sp.wait_ge(y_out, 16)

        @block.gpsimd
        def _(pool):
            nc.gpsimd.iota(table_base[:], pattern=[[0, TILES], [V, NF]], base=0,
                           channel_multiplier=0).then_inc(base_made, 1)
            with pool.Fori(0, TILES // 2) as pair:
                for half in range(2):
                    t = pair * 2 + half
                    pool.wait_ge(rows_ready, t + 1)
                    for s in range(NF):
                        c = s // 2
                        if s in FREE_AT:
                            pool.wait_ge(chunk_free, t * FIELD_CHUNKS + FREE_AT[s])
                            pool.sem_inc(pool_went_on, 1)
                        pool.indirect_dma_start(
                            out=gathered[:, s, :], out_offset=None, in_=tables,
                            in_offset=bass.IndirectOffsetOnAxis(ap=tile_rows[:, half, s:s + 1], axis=0),
                        ).then_inc(chunk_in[c], 16)

        @block.tensor
        def _(pe):
            pe.sem_inc(chunk_free, FIELD_CHUNKS)

            pe.wait_ge(dense_in, 16)
            nc.tensor.matmul(dense_mm1, dense_sb[0:ND, DENSE_W1:DENSE_W1 + D],
                             dense_sb[0:ND, DENSE_X:DENSE_X + B], start=True, stop=True).then_inc(dense_mm, 1)
            pe.wait_ge(dense_act, 1)
            nc.tensor.matmul(dense_mm2, dense_sb[:, DENSE_W2:DENSE_W2 + D],
                             dense_h[:], start=True, stop=True).then_inc(dense_mm, 1)
            pe.wait_ge(small_in, 16)

            def product_hi(hi, chunk, first=False):
                nc.tensor.matmul(acc[:], hi, w_hi[:, chunk, :], start=first, stop=False)
                nc.tensor.matmul(acc[:], hi, w_lo[:, chunk, :], start=False, stop=False)

            def product_lo(lo, chunk, last=False):
                return nc.tensor.matmul(acc[:], lo, w_hi[:, chunk, :], start=False, stop=last)

            def turn(t, c):
                pe.wait_ge(chunk_in[c], t * 32 + 32)
                if c >= 2:
                    pe.wait_ge(x_lo_done, t * FIELD_CHUNKS + c - 1)
                nc.tensor.transpose(turned[c % 2][:, 0:P], gathered[:, 2 * c:2 * c + 2, :]
                                    .rearrange("p f d -> p (f d)"), ident).then_inc(chunk_free, 1)

            def field_product(t, c):
                pe.wait_ge(x_lo_done, t * FIELD_CHUNKS + c + 1)
                product_hi(x_hi[:, c, :], c, first=(c == 0))
                product_lo(x_lo[:, c, :], c)

            def interactions(t):
                pe.wait_ge(emb_done, (t + 1) * NF)
                pe.wait_ge(dense_placed, t + 1)
                pe.sem_inc(pe_went_on, 1)
                for k in range(2):
                    for b in range(BANK_FROM[k], BANK_FROM[k + 1]):
                        j, n = b % 4, (b - BANK_FROM[k]) // 4
                        mm = nc.tensor.matmul(inter[k][QUAD * j:QUAD * j + PLACES, n * PLACES:(n + 1) * PLACES],
                                              emb[0:D, :, b], emb[0:D, :, b], start=True, stop=True)
                    mm.then_inc(inter_done, 1)

            def pair_product(t, part):
                pe.wait_ge(p_hi_done, t * PARTS + part + 1)
                for s in range(*SPLIT_SLOTS[part]):
                    product_hi(p_hi[:, s, :], FIELD_CHUNKS + s)
                pe.wait_ge(p_lo_done, t * PARTS + part + 1)
                for s in range(*SPLIT_SLOTS[part]):
                    mm = product_lo(p_lo[:, s, :], FIELD_CHUNKS + s, last=(s == SLOTS - 1))
                if part == PARTS - 1:
                    mm.then_inc(acc_done, 1)

            def z1_to_features(t):
                for step, (k0, k1) in enumerate(Z1_STEPS):
                    pe.wait_ge(z1_done, t * STEPS + step + 1)
                    for k in range(k0, k1):
                        mm = nc.tensor.transpose(z1_turned[step][:, (k - k0) * P:(k - k0 + 1) * P],
                                                 z1[:, k * P:(k + 1) * P], ident)
                    mm.then_inc(z1_turn, 1)

            def layer2(t, steps=range(STEPS)):
                for step in steps:
                    pe.wait_ge(z1t_done, t * STEPS + step + 1)
                    for m, k in LAYER2_STEPS[step]:
                        mm = nc.tensor.matmul(z2_ps[m], ow2[:, k, m * P:(m + 1) * P],
                                              z1t[:, k, :], start=(k == 0), stop=(k == H1 // P - 1))
                        if k == H1 // P - 1:
                            mm.then_inc(z2_mm, 1)

            def layer3(t):
                pe.wait_ge(z2_act, t + 1)
                nc.tensor.matmul(z3_ps, ow3[:, 0, :], z2t[:, 0, :], start=True, stop=False)
                pe.wait_ge(z2_dve, t + 1)
                nc.tensor.matmul(z3_ps, ow3[:, 1, :], z2t[:, 1, :], start=False, stop=True) \
                  .then_inc(z3_mm, 1)

            def layer4(t):
                pe.wait_ge(z3_act, t + 1)
                nc.tensor.matmul(y_ps, ow4, z3t[:], start=True, stop=True).then_inc(y_mm, 1)

            for c in range(AHEAD):
                turn(0, c)
            for c in range(AHEAD):
                pe.wait_ge(w_lo_done, c // W_GROUP + 1)
                field_product(0, c)
            pe.wait_ge(w_lo_done, W_GROUPS)

            def tile(t, first=False, last=False):
                for c in range(AHEAD, FIELD_CHUNKS):
                    turn(t, c)
                    if c - LAG >= AHEAD:
                        field_product(t, c - LAG)
                    if last and c in LAYER2_AT:
                        layer2(t - 1, LAYER2_AT[c])
                held = FIELD_CHUNKS - (2 if last else 1)
                for c in range(FIELD_CHUNKS - LAG, held):
                    field_product(t, c)
                interactions(t)
                for c in range(held, FIELD_CHUNKS):
                    field_product(t, c)
                if not first and not last:
                    layer2(t - 1)
                for part in range(PARTS):
                    if not last:
                        turn(t + 1, part)
                    pair_product(t, part)
                if not last:
                    turn(t + 1, PARTS)
                if not first:
                    layer3(t - 1)
                z1_to_features(t)
                if not last:
                    field_product(t + 1, 0)
                    for c in range(PARTS + 1, AHEAD):
                        turn(t + 1, c)
                    field_product(t + 1, 1)
                if not first:
                    layer4(t - 1)
                if not last:
                    for c in range(2, AHEAD):
                        field_product(t + 1, c)

            tile(FIRST, first=True)
            with pe.Fori(FIRST + 1, LAST) as t:
                tile(t)
            tile(LAST, last=True)
            layer2(LAST)
            layer3(LAST)
            layer4(LAST)

        @block.scalar
        def _(act):
            act.dma_start(dense_sb[:], dense_pack).then_inc(dense_in, 16)
            act.dma_start(small[:], small_pack).then_inc(small_in, 16)
            act.wait_ge(dense_in, 16)
            act.wait_ge(dense_mm, 1)
            nc.scalar.activation(dense_h[:], dense_mm1, ACT.Relu,
                                 bias=dense_sb[:, DENSE_B1:DENSE_B1 + 1]).then_inc(dense_act, 1)
            act.wait_ge(dense_mm, 2)
            nc.scalar.activation(dense_emb[:], dense_mm2, ACT.Relu,
                                 bias=dense_sb[:, DENSE_B2:DENSE_B2 + 1]).then_inc(dense_act, 1)

            def weights_hi(g):
                act.wait_ge(w_in[g % W_RING], 16 * (g // W_RING + 1))
                nc.scalar.activation(w_hi[:, g * W_GROUP:(g + 1) * W_GROUP, :], w_raw[:, g % W_RING],
                                     ACT.Copy).then_inc(w_hi_done, 1)

            for g in range(W_FIRST):
                weights_hi(g)
            act.wait_ge(small_in, 16)

            def keep(t, c):
                bank = turned[c % 2]
                act.wait_ge(chunk_free, t * FIELD_CHUNKS + FIELD_CHUNKS + c + 1)
                nc.scalar.activation(emb[:, place(2 * c), :], bank[:, 0:P], ACT.Copy).then_inc(emb_done, 1)
                nc.scalar.activation(emb[0:D, place(2 * c + 1), :], bank[D:P, 0:P], ACT.Copy) \
                  .then_inc(emb_done, 1)
                nc.scalar.activation(x_hi[:, c, :], bank[:, 0:P], ACT.Copy).then_inc(x_hi_done, 1)

            def dense_place(t):
                tile = bass.ds(t * P, P)
                nc.scalar.activation(emb[0:D, DENSE_PLACE, :], dense_emb[:, tile], ACT.Copy)
                nc.scalar.activation(pairs[0:D, SLOTS - 1, :], dense_emb[:, tile], ACT.Copy).then_inc(dense_placed, 1)

            def moves(t):
                for k in range(2):
                    act.wait_ge(inter_done, t * 2 + k + 1)
                    move(lambda dst, src: nc.scalar.activation(dst, src, ACT.Copy), k, (0, 1)) \
                        .then_inc(moved_act, 1)
                act.wait_ge(moved_act, t * 2 + 2)
                act.wait_ge(moved_dve, t * 2 + 2)

            def pairs_hi(part):
                slots = slice(*SPLIT_SLOTS[part])
                nc.scalar.activation(p_hi[:, slots, :], pairs[:, slots, :], ACT.Copy).then_inc(p_hi_done, 1)

            def z1_relu(t):
                act.wait_ge(acc_done, t + 1)
                for k0, k1 in Z1_STEPS:
                    nc.scalar.activation(z1[:, k0 * P:k1 * P], acc[:, k0 * P:k1 * P], ACT.Relu).then_inc(z1_done, 1)

            def z2_relu(t):
                act.wait_ge(z2_mm, t * 2 + 1)
                nc.scalar.activation(z2t[:, 0, :], z2_ps[0], ACT.Relu,
                                     bias=small[:, OB2:OB2 + 1]).then_inc(z2_act, 1)

            def z3_relu(t):
                act.wait_ge(z3_mm, t + 1)
                nc.scalar.activation(z3t[:], z3_ps, ACT.Relu,
                                     bias=small[:, OB3:OB3 + 1]).then_inc(z3_act, 1)

            def tile(t, first=False, last=False):
                for c in range(AHEAD, FIELD_CHUNKS):
                    keep(t, c)
                    if last and c == FIELD_CHUNKS - 1:
                        z2_relu(t - 1)
                moves(t)
                for part in range(PARTS):
                    pairs_hi(part)
                if not first and not last:
                    z2_relu(t - 1)
                if not last:
                    for c in range(PARTS):
                        keep(t + 1, c)
                z1_relu(t)
                if not first:
                    z3_relu(t - 1)
                if not last:
                    for c in range(PARTS, AHEAD):
                        keep(t + 1, c)
                    act.wait_ge(p_lo_done, (t + 1) * PARTS)
                    dense_place(t + 1)

            act.wait_ge(ones_set, 2)
            act.wait_ge(dense_act, 2)
            dense_place(FIRST)
            for c in range(AHEAD):
                keep(0, c)
            for g in range(W_FIRST, W_GROUPS):
                weights_hi(g)
            tile(FIRST, first=True)
            with act.Fori(FIRST + 1, LAST) as t:
                tile(t)
            tile(LAST, last=True)
            z2_relu(LAST)
            z3_relu(LAST)

        @block.vector
        def _(dve):
            dve.wait_ge(idx_in, 16)

            def row_numbers(n, tiles, to, done):
                nc.vector.tensor_scalar(idx_wrap[:, tiles, :], idx_raw[:, tiles, :], 0, V, ALU.is_lt, ALU.mult) \
                  .then_inc(idx_step, 1)
                dve.wait_ge(idx_step, n + 1)
                nc.vector.scalar_tensor_tensor(idx_pos[:, tiles, :], idx_raw[:, tiles, :], -V,
                                               idx_wrap[:, tiles, :], ALU.max, ALU.add).then_inc(idx_step, 1)
                dve.wait_ge(idx_step, n + 2)
                dve.wait_ge(base_made, 1)
                nc.vector.scalar_tensor_tensor(to, idx_pos[:, tiles, :], V - 1, table_base[:, tiles, :],
                                               ALU.min, ALU.add).then_inc(done, 1)

            row_numbers(0, slice(0, 1), tile_rows[:, 0:1, :], rows_ready)
            dve.wait_ge(later_idx_in, 16)
            row_numbers(2, slice(1, TILES), rows[:, 1:TILES, :], rows_done)
            nc.vector.memset(pairs[:], 1.0).then_inc(ones_set, 1)
            nc.vector.memset(emb[:, IDLE_PLACE, :], 0.0).then_inc(ones_set, 1)

            def weights_lo(g):
                dve.wait_ge(w_hi_done, g + 1)
                chunks = slice(g * W_GROUP, (g + 1) * W_GROUP)
                nc.vector.tensor_tensor(w_lo[:, chunks, :], w_raw[:, g % W_RING], w_hi[:, chunks, :],
                                        ALU.subtract).then_inc(w_lo_done, 1)

            for g in range(W_FIRST):
                weights_lo(g)
            dve.wait_ge(small_in, 16)

            def split(t, c):
                dve.wait_ge(x_hi_done, t * FIELD_CHUNKS + c + 1)
                nc.vector.tensor_tensor(x_lo[:, c, :], turned[c % 2][:, 0:P], x_hi[:, c, :], ALU.subtract) \
                  .then_inc(x_lo_done, 1)

            def moves(t):
                for k in range(2):
                    dve.wait_ge(inter_done, t * 2 + k + 1)
                    move(nc.vector.tensor_copy, k, (2, 3)).then_inc(moved_dve, 1)

            def pairs_lo(t, part):
                dve.wait_ge(p_hi_done, t * PARTS + part + 1)
                slots = slice(*SPLIT_SLOTS[part])
                nc.vector.tensor_tensor(p_lo[:, slots, :], pairs[:, slots, :], p_hi[:, slots, :],
                                        ALU.subtract).then_inc(p_lo_done, 1)

            def z1_features(t):
                for step, (k0, k1) in enumerate(Z1_STEPS):
                    dve.wait_ge(z1_turn, t * STEPS + step + 1)
                    nc.vector.tensor_copy(z1t[:, k0:k1, :], z1_turned[step].rearrange("p (k b) -> p k b", b=P)) \
                      .then_inc(z1t_done, 1)

            def z2_relu(t):
                dve.wait_ge(z2_mm, t * 2 + 2)
                nc.vector.tensor_scalar(z2t[:, 1, :], z2_ps[1], small[:, OB2 + 1:OB2 + 2], 0.0,
                                        ALU.add, ALU.max).then_inc(z2_dve, 1)

            def outputs(t):
                dve.wait_ge(y_mm, t + 1)
                nc.vector.tensor_scalar(y[:, bass.ds(t * P, P)], y_ps, small[0:1, OB4:OB4 + 1], None,
                                        ALU.add).then_inc(y_done, 1)

            def next_rows(t):
                nc.vector.tensor_copy(tile_rows[:, bass.ds((t + 1) % 2, 1), :], rows[:, bass.ds(t + 1, 1), :]) \
                  .then_inc(rows_ready, 1)

            def tile(t, first=False, last=False):
                if not last:
                    next_rows(t)
                for c in range(AHEAD, FIELD_CHUNKS):
                    split(t, c)
                    if last and c == FIELD_CHUNKS - 1:
                        z2_relu(t - 1)
                moves(t)
                for part in range(PARTS):
                    pairs_lo(t, part)
                if not first and not last:
                    z2_relu(t - 1)
                if not last:
                    for c in range(PARTS):
                        split(t + 1, c)
                z1_features(t)
                if not last:
                    split(t + 1, PARTS)
                if not first:
                    outputs(t - 1)
                if not last:
                    for c in range(PARTS + 1, AHEAD):
                        split(t + 1, c)

            for c in range(AHEAD):
                split(0, c)
            for g in range(W_FIRST, W_GROUPS):
                weights_lo(g)
            dve.wait_ge(rows_done, 1)
            tile(FIRST, first=True)
            with dve.Fori(FIRST + 1, LAST) as t:
                tile(t)
            tile(LAST, last=True)
            z2_relu(LAST)
            outputs(LAST)


def lay_out(inputs):
    import numpy as np

    def given(name):
        return np.asarray(inputs[name])

    ow1 = given("L0_rec_ow1")
    w1 = np.zeros((P, CHUNKS, H1), ow1.dtype)
    fields = ow1[D:NE * D].reshape(FIELD_CHUNKS, P, H1)
    w1[:, 0:FIELD_CHUNKS] = fields.transpose(1, 0, 2)
    places = [DENSE_PLACE, *SPARSE_PLACES]
    for g in range(1, NE):
        q, slot = divmod(places[g], SLOTS)
        for f in range(g):
            pair = NE * D + f * NE - f * (f + 1) // 2 + g - f - 1
            w1[QUAD * q + places[f], FIELD_CHUNKS + slot] = ow1[pair]
    w1[0:D, CHUNKS - 1] = ow1[0:D]
    w1[ONES_ROW, FIELD_CHUNKS] = given("L0_rec_ob1")

    dense_pack = np.zeros((D, DENSE_COLS), ow1.dtype)
    dense_pack[0:ND, DENSE_X:DENSE_X + B] = given("r_dense").T
    dense_pack[0:ND, DENSE_W1:DENSE_W1 + D] = given("L0_rec_dw1")
    dense_pack[:, DENSE_W2:DENSE_W2 + D] = given("L0_rec_dw2")
    dense_pack[:, DENSE_B1] = given("L0_rec_db1")
    dense_pack[:, DENSE_B2] = given("L0_rec_db2")

    small = np.zeros((P, SMALL_COLS), ow1.dtype)
    small[:, IDENT:IDENT + P] = np.eye(P, dtype=ow1.dtype)
    small[:, OW2:OW2 + 4 * H2] = given("L0_rec_ow2").reshape(4, P, H2).transpose(1, 0, 2).reshape(P, -1)
    small[:, OW3:OW3 + 2 * H3] = given("L0_rec_ow3").reshape(2, P, H3).transpose(1, 0, 2).reshape(P, -1)
    small[:, OW4:OW4 + 1] = given("L0_rec_ow4")
    small[:, OB2:OB2 + 2] = given("L0_rec_ob2").reshape(2, P).T
    small[:, OB3] = given("L0_rec_ob3")
    small[0, OB4] = given("L0_rec_ob4")[0]

    idx = given("r_sparse_idx").reshape(TILES, P, NF).transpose(1, 0, 2)
    return {
        "idx": np.ascontiguousarray(idx),
        "tables": given("L0_rec_emb_tables").reshape(NF * V, D),
        "dense_pack": dense_pack,
        "small_pack": small,
        "w1": w1,
    }


def kernel(**inputs):
    import concourse.bacc as bacc
    from concourse.bass_utils import run_bass_kernel_spmd

    nc = bacc.Bacc("TRN2", target_bir_lowering=False, num_devices=1)
    arrays = lay_out(inputs)
    args = [nc.dram_tensor(name, a.shape, mybir.dt.from_np(a.dtype), kind="ExternalInput").ap()
            for name, a in arrays.items()]
    out = nc.dram_tensor("out", (1, B), F32, kind="ExternalOutput").ap()
    build(nc, *args, out)
    got = run_bass_kernel_spmd(nc, [arrays], core_ids=[0])
    return got.results[0]["out"].reshape(B, 1)
```
